# Optimizing a Trainium2 kernel written in Bass

```python
import numpy as np
import jax
import jax.numpy as jnp

def _softmax(x, axis=-1):
    return jax.nn.softmax(x, axis=axis)

def _gelu(x):
    return jax.nn.gelu(x, approximate=True)

def _silu(x):
    return jax.nn.silu(x)

def _sigmoid(x):
    return jax.nn.sigmoid(x)

def _layernorm(x, axis=-1, eps=1e-05):
    m = jnp.mean(x, axis=axis, keepdims=True)
    v = jnp.var(x, axis=axis, keepdims=True)
    return (x - m) / jnp.sqrt(v + eps)

def _scatter_add(tgt, idx, src, axis=0):
    return tgt.at[idx].add(src)

def _segment_sum(src, seg, n):
    return jax.ops.segment_sum(src, seg, n)
kernel_name = 'mk_adaln_attn_ffn_d1_seqx_r8_7fe160'

def setup_inputs(seed: int=0):
    np.random.seed(seed)
    _w = jnp.asarray

    def _rec_inputs():
        import jax
        import jax.numpy as jnp
        _rk = jax.random.key(seed)
        x = -7.109e-05 + 0.9999 * jax.random.normal(jax.random.fold_in(_rk, 1), (128, 32, 512), jnp.float32)
        _lenS = 32 - jax.random.randint(jax.random.fold_in(_rk, 7), (128,), 0, max(1, 32 // 4) + 1, jnp.int32)
        _lenS2 = 32 - jax.random.randint(jax.random.fold_in(_rk, 8), (128,), 0, max(1, 32 // 4) + 1, jnp.int32)
        itok_B_0_15 = jax.random.randint(jax.random.fold_in(_rk, 11), (128,), 0, 16, jnp.int32)
        itok_B_8_3872 = jax.random.randint(jax.random.fold_in(_rk, 12), (128,), 8, 3873, jnp.int32)
        return (x, itok_B_0_15, itok_B_8_3872)
    x, itok_B_0_15, itok_B_8_3872 = _rec_inputs()

    def _L0_cond_setup():
        import jax, jax.numpy as jnp
        import numpy as np
        B, C, T = (64, 32, 512)
        S, D = (16, 32)
        key = jax.random.key(seed)
        k1, k2, k3 = jax.random.split(key, 3)
        x = jax.random.normal(k1, (B, C, T), dtype=jnp.float32)
        condition = jax.random.randint(k2, (B,), 0, S, dtype=jnp.int64)
        bound = float(np.sqrt(6.0 / C))
        weights = jax.random.uniform(k3, (S, C, D), dtype=jnp.float32, minval=-bound, maxval=bound)
        return {'x': x, 'condition': condition, 'weights': weights}
    _L0_cond_all = _L0_cond_setup()
    _L0_cond_in = {k: v for k, v in _L0_cond_all.items() if k in ('weights',)}
    del _L0_cond_all

    def _L0_attn_setup():
        import jax, jax.numpy as jnp
        import numpy as np
        B, S, H = (1, 256, 512)
        NH = 32
        Q_LORA, KV_LORA = (192, 64)
        QK_NOPE, QK_ROPE = (128, 64)
        Q_HEAD = QK_NOPE + QK_ROPE
        V_HEAD = 128
        key = jax.random.key(seed)
        ks = jax.random.split(key, 12)

        def lin(k, out_d, in_d):
            s = 1.0 / np.sqrt(in_d)
            return jax.random.uniform(k, (out_d, in_d), jnp.float32, -s, s)
        return {'hidden_size': jax.random.normal(ks[0], (B, S, H), jnp.float32), 'Wq_c': lin(ks[1], Q_LORA, H), 'bq_c': jnp.zeros((Q_LORA,), jnp.float32), 'Wq_up': lin(ks[2], NH * Q_HEAD, Q_LORA), 'bq_up': jnp.zeros((NH * Q_HEAD,), jnp.float32), 'Wkv_c': lin(ks[3], KV_LORA + QK_ROPE, H), 'bkv_c': jnp.zeros((KV_LORA + QK_ROPE,), jnp.float32), 'Wkv_up': lin(ks[4], NH * (QK_NOPE + V_HEAD), KV_LORA), 'bkv_up': jnp.zeros((NH * (QK_NOPE + V_HEAD),), jnp.float32), 'Wo': lin(ks[5], H, V_HEAD), 'bo': jnp.zeros((H,), jnp.float32)}
    _L0_attn_all = _L0_attn_setup()
    _L0_attn_in = {k: v for k, v in _L0_attn_all.items() if k in ('Wq_c', 'bq_c', 'Wq_up', 'bq_up', 'Wkv_c', 'bkv_c', 'Wkv_up', 'bkv_up', 'Wo', 'bo')}
    del _L0_attn_all

    def _L0_cond2_setup():
        import math
        import jax, jax.numpy as jnp
        import numpy as np
        H, N, B, L = (32, 64, 16, 512)
        DT_MIN, DT_MAX = (0.001, 0.1)

        def _get_kernel(log_dt, C, log_A_real, A_imag, length):
            Cc = C[..., 0] + 1j * C[..., 1]
            dt = jnp.exp(log_dt)
            A = -jnp.exp(log_A_real) + 1j * A_imag
            dtA = A * dt[:, None]
            P = dtA[:, :, None] * jnp.arange(length, dtype=jnp.float32)
            Cs = Cc * (jnp.exp(dtA) - 1.0) / A
            K = 2.0 * jnp.einsum('hn,hnl->hl', Cs, jnp.exp(P)).real
            return K
        key = jax.random.key(seed)
        ks = jax.random.split(key, 6)
        u = jax.random.normal(ks[0], (B, H, L), dtype=jnp.float32)
        length = jax.random.randint(ks[1], (B,), 0, L)
        log_dt = jax.random.uniform(ks[2], (H,), dtype=jnp.float32) * (math.log(DT_MAX) - math.log(DT_MIN)) + math.log(DT_MIN)
        C = jax.random.normal(ks[3], (H, N, 2), dtype=jnp.float32)
        log_A_real = jnp.log(0.5 * jnp.ones((H, N), dtype=jnp.float32))
        A_imag = math.pi * jnp.broadcast_to(jnp.arange(N, dtype=jnp.float32), (H, N))
        D = jax.random.normal(ks[4], (H,), dtype=jnp.float32)
        return {'u': u, 'length': length, 'log_dt': log_dt, 'C': C, 'log_A_real': log_A_real, 'A_imag': A_imag, 'D': D}
    _L0_cond2_all = _L0_cond2_setup()
    _L0_cond2_in = {k: v for k, v in _L0_cond2_all.items() if k in ('log_dt', 'C', 'log_A_real', 'A_imag', 'D')}
    del _L0_cond2_all

    def _L0_ffn_setup():
        import jax, jax.numpy as jnp
        import numpy as np
        IN_FEATURES = 512

        def _dequantize(qweight, scale, zero_point):
            N, K_packed = qweight.shape
            groups = K_packed // 3
            p = qweight.reshape(N, groups, 3)
            v0 = p[:, :, 0] & 63
            v1 = p[:, :, 0] >> 6 & 63
            v2 = p[:, :, 1] & 63
            v3 = p[:, :, 2] & 63
            unpacked = jnp.stack([v0, v1, v2, v3], axis=2).reshape(N, groups * 4)
            unpacked = unpacked[:, :IN_FEATURES]
            return (unpacked.astype(jnp.float32) - zero_point) * scale
        key = jax.random.key(seed)
        k1, k2, k3, k4, k5 = jax.random.split(key, 5)
        x = jax.random.normal(k1, (8, 256, 512), dtype=jnp.float32)
        qweight = jax.random.randint(k2, (512, 384), 0, 512, dtype=jnp.int32)
        weight_scale = jax.random.uniform(k3, (512, 1), dtype=jnp.float32) * 0.02 + 0.001
        weight_zero_point = jax.random.uniform(k4, (512, 1), dtype=jnp.float32) * 63.0
        bias = jax.random.normal(k5, (512,), dtype=jnp.float32)
        return {'x': x, 'qweight': qweight, 'weight_scale': weight_scale, 'weight_zero_point': weight_zero_point, 'bias': bias}
    _L0_ffn_all = _L0_ffn_setup()
    _L0_ffn_in = {k: v for k, v in _L0_ffn_all.items() if k in ('qweight', 'weight_scale', 'weight_zero_point', 'bias')}
    del _L0_ffn_all
    return {'x': x, 'itok_B_0_15': itok_B_0_15, 'itok_B_8_3872': itok_B_8_3872, 'L0_cond_weights': _L0_cond_in['weights'], 'L0_attn_Wq_c': _L0_attn_in['Wq_c'], 'L0_attn_bq_c': _L0_attn_in['bq_c'], 'L0_attn_Wq_up': _L0_attn_in['Wq_up'], 'L0_attn_bq_up': _L0_attn_in['bq_up'], 'L0_attn_Wkv_c': _L0_attn_in['Wkv_c'], 'L0_attn_bkv_c': _L0_attn_in['bkv_c'], 'L0_attn_Wkv_up': _L0_attn_in['Wkv_up'], 'L0_attn_bkv_up': _L0_attn_in['bkv_up'], 'L0_attn_Wo': _L0_attn_in['Wo'], 'L0_attn_bo': _L0_attn_in['bo'], 'L0_cond2_log_dt': _L0_cond2_in['log_dt'], 'L0_cond2_C': _L0_cond2_in['C'], 'L0_cond2_log_A_real': _L0_cond2_in['log_A_real'], 'L0_cond2_A_imag': _L0_cond2_in['A_imag'], 'L0_cond2_D': _L0_cond2_in['D'], 'L0_ffn_qweight': _L0_ffn_in['qweight'], 'L0_ffn_weight_scale': _L0_ffn_in['weight_scale'], 'L0_ffn_weight_zero_point': _L0_ffn_in['weight_zero_point'], 'L0_ffn_bias': _L0_ffn_in['bias']}

def reference(x, itok_B_0_15, itok_B_8_3872, L0_cond_weights, L0_attn_Wq_c, L0_attn_bq_c, L0_attn_Wq_up, L0_attn_bq_up, L0_attn_Wkv_c, L0_attn_bkv_c, L0_attn_Wkv_up, L0_attn_bkv_up, L0_attn_Wo, L0_attn_bo, L0_cond2_log_dt, L0_cond2_C, L0_cond2_log_A_real, L0_cond2_A_imag, L0_cond2_D, L0_ffn_qweight, L0_ffn_weight_scale, L0_ffn_weight_zero_point, L0_ffn_bias):
    import jax
    import jax.numpy as jnp

    def _L0_cond_ref(x, condition, weights):
        import jax, jax.numpy as jnp
        import numpy as np
        B, C, T = (64, 32, 512)
        S, D = (16, 32)
        W = weights[condition]
        return jnp.einsum('bct,bcd->bdt', x, W)

    def _L0_attn_ref(hidden_size, Wq_c, bq_c, Wq_up, bq_up, Wkv_c, bkv_c, Wkv_up, bkv_up, Wo, bo):
        import jax, jax.numpy as jnp
        import numpy as np
        B, S, H = (1, 256, 512)
        NH = 32
        Q_LORA, KV_LORA = (192, 64)
        QK_NOPE, QK_ROPE = (128, 64)
        Q_HEAD = QK_NOPE + QK_ROPE
        V_HEAD = 128
        b, s, _ = hidden_size.shape
        q_c = hidden_size @ Wq_c.T + bq_c
        q = (q_c @ Wq_up.T + bq_up).reshape(b, s, NH, Q_HEAD).transpose(0, 2, 1, 3)
        kv = hidden_size @ Wkv_c.T + bkv_c
        kv_nope, kv_rope = (kv[..., :KV_LORA], kv[..., KV_LORA:])
        kvu = (kv_nope @ Wkv_up.T + bkv_up).reshape(b, s, NH, QK_NOPE + V_HEAD).transpose(0, 2, 1, 3)
        k_nope, v = (kvu[..., :QK_NOPE], kvu[..., QK_NOPE:])
        k_rope = jnp.broadcast_to(kv_rope[:, None, :, :], (b, NH, s, QK_ROPE))
        k = jnp.concatenate([k_nope, k_rope], axis=-1)
        scores = jnp.einsum('bhqd,bhkd->bhqk', q, k) / np.sqrt(Q_HEAD)
        attn = jax.nn.softmax(scores, axis=-1)
        o = jnp.einsum('bhqk,bhkv->bhqv', attn, v)
        out = jnp.einsum('bhsv,Hv->bsH', o, Wo) + bo
        return out

    def _L0_cond2_ref(u, length, log_dt, C, log_A_real, A_imag, D):
        import math
        import jax, jax.numpy as jnp
        import numpy as np
        H, N, B, L = (32, 64, 16, 512)
        DT_MIN, DT_MAX = (0.001, 0.1)

        def _get_kernel(log_dt, C, log_A_real, A_imag, length):
            Cc = C[..., 0] + 1j * C[..., 1]
            dt = jnp.exp(log_dt)
            A = -jnp.exp(log_A_real) + 1j * A_imag
            dtA = A * dt[:, None]
            P = dtA[:, :, None] * jnp.arange(length, dtype=jnp.float32)
            Cs = Cc * (jnp.exp(dtA) - 1.0) / A
            K = 2.0 * jnp.einsum('hn,hnl->hl', Cs, jnp.exp(P)).real
            return K
        Bq, Hq, Lq = u.shape
        mask = (jnp.arange(Lq) < length[:, None]).astype(u.dtype)
        u_m = u * mask[:, None, :]
        kernel = _get_kernel(log_dt, C, log_A_real, A_imag, Lq)
        n = 2 * Lq
        k_f = jnp.fft.rfft(kernel, n=n)
        u_f = jnp.fft.rfft(u_m, n=n)
        y = jnp.fft.irfft(u_f * k_f, n=n)[..., :Lq]
        y = y + u_m * D[:, None]
        return y * mask[:, None, :]

    def _L0_ffn_ref(x, qweight, weight_scale, weight_zero_point, bias):
        import jax, jax.numpy as jnp
        import numpy as np
        IN_FEATURES = 512

        def _dequantize(qweight, scale, zero_point):
            N, K_packed = qweight.shape
            groups = K_packed // 3
            p = qweight.reshape(N, groups, 3)
            v0 = p[:, :, 0] & 63
            v1 = p[:, :, 0] >> 6 & 63
            v2 = p[:, :, 1] & 63
            v3 = p[:, :, 2] & 63
            unpacked = jnp.stack([v0, v1, v2, v3], axis=2).reshape(N, groups * 4)
            unpacked = unpacked[:, :IN_FEATURES]
            return (unpacked.astype(jnp.float32) - zero_point) * scale
        w = _dequantize(qweight, weight_scale, weight_zero_point)
        return jnp.einsum('bsk,nk->bsn', x, w) + bias
    x = x + _L0_attn_ref(_L0_cond_ref(x, itok_B_0_15, L0_cond_weights), L0_attn_Wq_c, L0_attn_bq_c, L0_attn_Wq_up, L0_attn_bq_up, L0_attn_Wkv_c, L0_attn_bkv_c, L0_attn_Wkv_up, L0_attn_bkv_up, L0_attn_Wo, L0_attn_bo)
    x = x + _L0_ffn_ref(_L0_cond2_ref(x, itok_B_8_3872, L0_cond2_log_dt, L0_cond2_C, L0_cond2_log_A_real, L0_cond2_A_imag, L0_cond2_D), L0_ffn_qweight, L0_ffn_weight_scale, L0_ffn_weight_zero_point, L0_ffn_bias)
    return x

_drawn_inputs = setup_inputs


def setup_inputs(seed=0):
    import zlib

    import numpy as np

    out = dict(_drawn_inputs(seed))
    spreads = {'L0_attn_bq_c': (0.0, 0.593),
     'L0_attn_bq_up': (0.0, 0.314),
     'L0_attn_bkv_c': (0.0, 0.1),
     'L0_attn_bkv_up': (0.0, 0.1),
     'L0_attn_bo': (0.0, 0.1),
     'L0_cond2_log_A_real': (-0.6931471824645996, 0.2)}
    factors = {}
    for name, (base, spread) in spreads.items():
        noise = np.random.default_rng([zlib.crc32(name.encode()), seed]).standard_normal(out[name].shape)
        drawn = base * np.exp(spread * noise) if base else spread * noise
        out[name] = jnp.asarray(drawn.astype(out[name].dtype))
    for name, factor in factors.items():
        out[name] = (out[name] * factor).astype(out[name].dtype)
    return out
```

```python
from contextlib import ExitStack
import math

import concourse.bass as bass
from concourse import mybir

F32 = mybir.dt.float32
F32R = mybir.dt.float32r
I32 = mybir.dt.int32
ALU = mybir.AluOpType
ACT = mybir.ActivationFunctionType
AX = mybir.AxisListType

P = 128
B, C, T = 128, 32, 512
NH = 32
QL, KVL, NOPE, ROPE, VH = 192, 64, 128, 64, 128
QH = NOPE + ROPE
NCOND = 16
NMODE = 64
TT = T // P
CB = 8
CT = CB * C
NCH = B // CB
QUADS = NH // 4
NPAIR = NH // 2
SCALE = 1.0 / math.sqrt(QH)
HALF = T // 2

MAGIC = 1.5 * 2.0 ** 23
LOG2E = 1.0 / math.log(2.0)
LN2_HI = 0.693359375
LN2_LO = math.log(2.0) - LN2_HI
INV_2PI = 1.0 / (2.0 * math.pi)
PI_HI = 6.28125
PI_MID = math.floor((2 * math.pi - PI_HI) * 2.0 ** 20) / 2.0 ** 20
PI_LO = 2 * math.pi - PI_HI - PI_MID
PI_IN = 3.1415925
LA, LC = 16, 32
KPAD = 127
KROW = KPAD + T + 1


class Memory:

    def __init__(self, nc):
        self.nc, self.ctx = nc, ExitStack()

    def sb(self, name, shape, dt=F32):
        return self.ctx.enter_context(self.nc.sbuf_tensor(name, shape, dt))

    def sem(self, name):
        return self.ctx.enter_context(self.nc.semaphore(name))

    def free(self):
        self.ctx.close()


def f(ap):
    return ap.bitcast(F32)


def attention_weights(nc, d, w, ps, scratch):
    m = Memory(nc)
    wq_nope = m.sb("wq_nope", [P, NH, QL])
    wq_rope = m.sb("wq_rope", [ROPE, NH, QL])
    wk = m.sb("wk", [P, NH, KVL])
    wv = m.sb("wv", [P, NH, KVL])
    wc_raw = m.sb("wc_raw", [P, 3, T])
    bq_raw = m.sb("bq_raw", [NH, QH])
    bkv_raw = m.sb("bkv_raw", [NH, NOPE + VH])
    bq_nope = m.sb("bq_nope", [P, NH])
    cond_all = m.sb("cond_all", [NCOND, B], I32)
    cond_f = m.sb("cond_f", [NCOND, B])
    one_hot = m.sb("one_hot", [NCOND, B])
    row_id = m.sb("row_id", [NCOND, 1])
    mix_w = m.sb("mix_w", [NCOND, C * C])
    mixed = m.sb("mixed", [B, C * C])
    ones = m.sb("ones", [NH, 1])

    wc_in, wq_in0, wq_in1, wk_in, wv_in, bias_in, cond_in = (
        m.sem(n) for n in ("wc_in", "wq_in0", "wq_in1", "wk_in", "wv_in", "bias_in", "cond_in"))
    ident_ready = m.sem("ident_ready")
    const_ready = m.sem("const_ready")
    wcT_ready, wcT_high, wcT_done = (m.sem(n) for n in ("wcT_ready", "wcT_high", "wcT_done"))
    fold_ready, fold_high, fold_done = (m.sem(n) for n in ("fold_ready", "fold_high", "fold_done"))
    wvT_ready, wvT_high, wvT_done = (m.sem(n) for n in ("wvT_ready", "wvT_high", "wvT_done"))
    hot_step, hot_ready, mix_ready, mix_copied, mix_stored = (
        m.sem(n) for n in ("hot_step", "hot_ready", "mix_ready", "mix_copied", "mix_stored"))
    bq_turned, bq_copied, bias_ready, bias_done = (
        m.sem(n) for n in ("bq_turned", "bq_copied", "bias_ready", "bias_done"))

    with nc.Block() as block:

        @block.sync
        def _(sp):
            wq_c, wkv_c = d["L0_attn_Wq_c"], d["L0_attn_Wkv_c"]
            sp.dma_start(wc_raw[:, 0, :], wq_c[0:P, :]).then_inc(wc_in, 16)
            sp.dma_start(wc_raw[0:64, 1, :], wq_c[P:QL, :]).then_inc(wc_in, 16)
            sp.dma_start(wc_raw[64:P, 1, :], wq_c[P:QL, :]).then_inc(wc_in, 16)
            sp.dma_start(wc_raw[:, 2, :], wkv_c).then_inc(wc_in, 16)
            wkv = d["L0_attn_Wkv_up"].rearrange("(h n) c -> n h c", h=NH)
            sp.dma_start(wk[:], wkv[0:NOPE]).then_inc(wk_in, 16)
            wq = d["L0_attn_Wq_up"].rearrange("(h n) c -> n h c", h=NH)
            for n in range(2):
                hs = slice(n * NH // 2, (n + 1) * NH // 2)
                sp.dma_start(wq_nope[:, hs, :], wq[0:NOPE, hs]).then_inc((wq_in0, wq_in1)[n], 16)
                sp.dma_start(wq_rope[:, hs, :], wq[NOPE:QH, hs]).then_inc((wq_in0, wq_in1)[n], 16)
            sp.dma_start(wv[:], wkv[NOPE:NOPE + VH]).then_inc(wv_in, 16)

        @block.gpsimd
        def _(pool):
            pool.memset(w["ident"][:], 0.0).then_inc(ident_ready, 1)
            pool.memset(ones[:], 1.0).then_inc(const_ready, 1)
            pool.memset(w["mix"][:], 0.0).then_inc(const_ready, 1)
            pool.memset(w["c_high"][:].bitcast(F32), 0.0).then_inc(const_ready, 1)
            pool.memset(w["c_low"][:].bitcast(F32), 0.0).then_inc(const_ready, 1)
            pool.iota(row_id[:], pattern=[[0, 1]], base=0, channel_multiplier=1,
                      allow_small_or_imprecise_dtypes=True).then_inc(const_ready, 1)
            pool.wait_ge(ident_ready, 1)
            pool.affine_select(out=w["ident"][:], in_=w["ident"][:], compare_op=ALU.not_equal, fill=1.0,
                               base=0, pattern=[[-1, P]], channel_multiplier=1).then_inc(ident_ready, 1)
            pool.wait_ge(mix_copied, 2)
            pool.dma_start(scratch["mix"], mixed[:]).then_inc(mix_stored, 16)
            pool.wait_ge(mix_stored, 16)

        @block.tensor
        def _(pe):
            pe.wait_ge(ident_ready, 2)
            pe.wait_ge(wc_in, 64)
            for m_ in range(3):
                for t in range(TT):
                    mm = pe.transpose(ps[:, m_, t * P:(t + 1) * P], wc_raw[:, m_, t * P:(t + 1) * P],
                                      w["ident"][:])
                mm.then_inc(wcT_ready, 1)
            pe.wait_ge(hot_ready, 1)
            for n in range(2):
                pe.matmul(ps[:, 3, :] if n == 0 else ps[:, 4, :], one_hot[:],
                          mix_w[:, n * HALF * 2:(n + 1) * HALF * 2], start=True, stop=True).then_inc(mix_ready, 1)
            pe.wait_ge(wk_in, 16)
            pe.wait_ge(mix_copied, 2)
            for g in range(QUADS):
                if g == 0:
                    pe.wait_ge(wq_in0, 32)
                if g == QUADS // 2:
                    pe.wait_ge(wq_in1, 32)
                a, b = 4 + 2 * (g % 2), 5 + 2 * (g % 2)
                if g >= 2:
                    pe.wait_ge(fold_done, 2 * (g - 1))
                for j in range(4):
                    h = 4 * g + j
                    lat, rope = slice(j * P, j * P + 64), slice(j * P + 64, (j + 1) * P)
                    pe.matmul(ps[:, a, lat], wq_nope[:, h, 0:P], wk[:, h, :], start=True, stop=True)
                    pe.matmul(ps[:, a, rope], wq_rope[:, h, 0:P], w["ident"][0:64, 0:64], start=True, stop=True)
                    for half in (0, 64):
                        out = ps[half:half + 64, b, :]
                        pe.matmul(out[:, lat], wq_nope[:, h, P:QL], wk[:, h, :], start=True, stop=True)
                        mm = pe.matmul(out[:, rope], wq_rope[:, h, P:QL], w["ident"][0:64, 0:64],
                                       start=True, stop=True)
                mm.then_inc(fold_ready, 1)
            pe.wait_ge(wv_in, 16)
            pe.wait_ge(wcT_done, 3)
            pe.wait_ge(const_ready, 1)
            for p in range(NPAIR):
                mm = pe.transpose(ps[:, p // 4, (p % 4) * P:(p % 4 + 1) * P],
                                  wv[:, 2 * p:2 * p + 2, :].rearrange("v h c -> v (h c)"), w["ident"][:])
                if p % 4 == 3:
                    mm.then_inc(wvT_ready, 1)
            pe.wait_ge(bias_in, 16 * 6)
            pe.wait_ge(fold_done, 2 * QUADS)
            pe.transpose(ps[:, 7, 0:NH], bq_raw[:, 0:NOPE], w["ident"][0:NH, 0:NH]).then_inc(bq_turned, 1)
            pe.wait_ge(bq_copied, 1)
            for h in range(NH):
                pe.matmul(ps[0:64, 7, 64 + h:65 + h], wk[:, h, :], bq_nope[:, h:h + 1], start=True, stop=True)
            pe.matmul(ps[64:P, 7, 64:64 + NH], bq_raw[:, NOPE:QH], w["ident"][0:NH, 0:NH], start=True, stop=True)
            pe.matmul(ps[:, 7, 100:101], bkv_raw[:, NOPE:NOPE + VH], ones[:], start=True,
                      stop=True).then_inc(bias_ready, 1)

        @block.scalar
        def _(act):
            act.dma_start(cond_all[:], d["itok_B_0_15"].partition_broadcast(NCOND)).then_inc(cond_in, 16)
            act.dma_start(mix_w[:], d["L0_cond_weights"].rearrange("s c d -> s (c d)")).then_inc(cond_in, 16)
            col = lambda ap: ap.rearrange("(p a) -> p a", a=1)
            act.dma_start(bq_raw[:], d["L0_attn_bq_up"].rearrange("(h n) -> h n", h=NH)).then_inc(bias_in, 16)
            act.dma_start(bkv_raw[:], d["L0_attn_bkv_up"].rearrange("(h n) -> h n", h=NH)).then_inc(bias_in, 16)
            act.dma_start(w["bq_c"][:, 0:1], col(d["L0_attn_bq_c"][0:P])).then_inc(bias_in, 16)
            act.dma_start(w["bq_c"][0:64, 1:2], col(d["L0_attn_bq_c"][P:QL])).then_inc(bias_in, 16)
            act.dma_start(w["bq_c"][64:P, 1:2], col(d["L0_attn_bq_c"][P:QL])).then_inc(bias_in, 16)
            act.dma_start(w["bkv_c"][:], col(d["L0_attn_bkv_c"])).then_inc(bias_in, 16)
            for m_ in range(3):
                act.wait_ge(wcT_ready, m_ + 1)
                act.copy(w["wcT_high"][:, :, m_, :], ps[:, m_, :].rearrange("p (t n) -> p t n", t=TT)).then_inc(wcT_high, 1)
            for g in range(QUADS):
                a, b = 4 + 2 * (g % 2), 5 + 2 * (g % 2)
                act.wait_ge(fold_ready, g + 1)
                act.copy(w["m0_high"][:, g, :], ps[:, a, :]).then_inc(fold_high, 1)
                act.copy(w["m1"][:, g, :], ps[:, b, :]).then_inc(fold_high, 1)
            for n in range(4):
                act.wait_ge(wvT_ready, n + 1)
                act.copy(w["wvT_high"][:, 4 * n:4 * n + 4, :].rearrange("p a n -> p (a n)"), ps[:, n, :]).then_inc(wvT_high, 1)

        @block.vector
        def _(dve):
            dve.wait_ge(cond_in, 32)
            dve.wait_ge(const_ready, 5)
            dve.tensor_copy(cond_f[:], cond_all[:]).then_inc(hot_step, 1)
            dve.wait_ge(hot_step, 1)
            dve.tensor_scalar(one_hot[:], cond_f[:], row_id[:, 0:1], None, ALU.is_equal).then_inc(hot_ready, 1)
            for m_ in range(3):
                dve.wait_ge(wcT_high, m_ + 1)
                dve.tensor_tensor(w["wcT_low"][:, :, m_, :], ps[:, m_, :].rearrange("p (t n) -> p t n", t=TT),
                                  f(w["wcT_high"][:, :, m_, :]), ALU.subtract).then_inc(wcT_done, 1)
            for n in range(2):
                dve.wait_ge(mix_ready, n + 1)
                dve.tensor_copy(mixed[:, n * T:(n + 1) * T], ps[:, 3 + n, :]).then_inc(mix_copied, 1)
            for g in range(QUADS):
                a, b = 4 + 2 * (g % 2), 5 + 2 * (g % 2)
                dve.wait_ge(fold_high, 2 * g + 2)
                dve.tensor_tensor(w["m0_low"][:, g, :], ps[:, a, :], f(w["m0_high"][:, g, :]),
                                  ALU.subtract).then_inc(fold_done, 1)
                dve.tensor_tensor(w["m1"][64:P, g, :], ps[64:P, b, :], f(w["m1"][64:P, g, :]),
                                  ALU.subtract).then_inc(fold_done, 1)
            for n in range(4):
                dve.wait_ge(wvT_high, n + 1)
                dve.tensor_tensor(w["wvT_low"][:, 4 * n:4 * n + 4, :].rearrange("p a n -> p (a n)"), ps[:, n, :],
                                  f(w["wvT_high"][:, 4 * n:4 * n + 4, :].rearrange("p a n -> p (a n)")),
                                  ALU.subtract).then_inc(wvT_done, 1)
            dve.wait_ge(bq_turned, 1)
            dve.tensor_copy(bq_nope[:], ps[:, 7, 0:NH]).then_inc(bq_copied, 1)
            dve.wait_ge(bias_ready, 1)
            dve.tensor_copy(w["m_bias"][:], ps[:, 7, 64:64 + NH]).then_inc(bias_done, 1)
            dve.tensor_copy(w["bv_sum"][:], ps[:, 7, 100:101]).then_inc(bias_done, 1)
            dve.wait_ge(bias_done, 2)
            dve.wait_ge(wvT_done, 4)
            dve.wait_ge(fold_done, 2 * QUADS)

    m.free()


def attention(nc, d, w, ps, scratch):
    m = Memory(nc)
    x_in = m.sb("x_in", [P, 2, T])
    q0_high = m.sb("q0_high", [P, CT], F32R)
    q0_low = m.sb("q0_low", [P, CT], F32R)
    q1_high = m.sb("q1_high", [P, CT], F32R)
    q1_low = m.sb("q1_low", [P, CT], F32R)
    kv = m.sb("kv", [P, CT])
    qt = m.sb("qt", [P, NH, CT])
    sc = m.sb("sc", [P, CB, QUADS, C])
    pT_low = m.sb("pT_low", [P, CB, QUADS, C], F32R)
    pT_high = m.sb("pT_high", [P, CB, QUADS, C], F32R)
    z_high = m.sb("z_high", [P, 2, QUADS, CT], F32R)
    z_low_at = -(-nc.sbuf_base // 32) * 32
    z_low = m.sb("z_low", [P, 2, QUADS, CT], F32R)
    assert nc.sbuf_base == z_low_at + 4 * 2 * QUADS * CT
    h_high = z_low[:, 0, 0:4, :]
    h_low = z_low[:, 0, 4:8, :]
    ctok = z_low[:, 1, 0, :].rearrange("p (a g c) -> p a g c", a=2, g=2)
    pT = nc.alloc_sbuf_tensor_at("pT", [P, CB, QUADS, C], F32, offset=z_low_at)
    row_max = m.sb("row_max", [P, CB, QUADS])
    row_sum = m.sb("row_sum", [P, CB, QUADS])
    row_inv = m.sb("row_inv", [P, CB, QUADS])

    names = ("x_loaded mix_loaded c_stored c_loaded h_ready h_high_done h_low_done q_ready kv_ready "
             "q_high_done q_done kv_done ct_ready ct_high_done ct_done t_ready qt_done s_ready s_taken max_done "
             "sub_done exp_done sum_done inv_done norm_done turn_done ph_done pl_done z_ready zh_done zl_done "
             "o_ready o_done").split()
    s = {n: m.sem(n) for n in names}
    BT0, BS0, BZ0, BO, BX = 0, 2, 4, 6, 7
    SP = CB // 2

    with nc.Block() as block:

        @block.sync
        def _(sp):
            x_v = d["x"].rearrange("(g b) c t -> (b c) g t", b=4)
            mix_v = scratch["mix"].rearrange("(g b) (c e) -> b c g e", b=4, c=C)
            c_st = scratch["lat"].rearrange("(g p) a c -> p a g c", p=P)

            def load_x(i):
                sp.dma_start(x_in[:], x_v[:, bass.ts(i, 2), :]).then_inc(s["x_loaded"], 16)
                for b in range(4):
                    rows = slice(32 * b, 32 * b + 32)
                    sp.dma_start(w["mix"][rows, :, rows], mix_v[b, :, bass.ts(i, 2), :]).then_inc(s["mix_loaded"], 16)

            def store_latent(i):
                sp.wait_ge(s["ct_done"], 1 * i + 1)
                sp.dma_start(c_st[:, :, bass.ts(i, 2), :], f(ctok)).then_inc(s["c_stored"], 16)

            load_x(0)
            sp.wait_ge(s["h_ready"], 2)
            load_x(1)
            store_latent(0)

            def body(i):
                sp.wait_ge(s["h_ready"], 2 * i + 2)
                load_x(i + 1)
                store_latent(i)

            with sp.Fori(1, NCH - 1) as i:
                body(i)
            store_latent(NCH - 1)

        @block.gpsimd
        def _(pool):
            c_ld = scratch["lat"].rearrange("(b k) a c -> a k b c", k=C)

            def load_latent(i, first=False):
                pool.wait_ge(s["c_stored"], 16 * i + 16)
                if not first:
                    pool.wait_ge(s["z_ready"], CB * i)
                for a, tile in ((0, w["c_high"]), (1, w["c_low"])):
                    for j in range(4):
                        pool.dma_start(f(tile[32 * j:32 * j + 32, :, j // 2, 64 * (j % 2):64 * (j % 2) + 64]),
                                       c_ld[a, :, bass.ts(i, CB), :]).then_inc(s["c_loaded"], 16)

            load_latent(0, True)
            with pool.Fori(1, NCH) as i:
                load_latent(i)

        @block.tensor
        def _(pe):
            def three(out, lh, ll, rh, rl, start=True, stop=True):
                pe.matmul(out, lh, rh, start=start, stop=False)
                pe.matmul(out, lh, rl, start=False, stop=False)
                return pe.matmul(out, ll, rh, start=False, stop=stop)

            def front(i, first):
                pe.wait_ge(s["x_loaded"], 16 * i + 16)
                pe.wait_ge(s["mix_loaded"], 64 * i + 64)
                if not first:
                    pe.wait_ge(s["s_taken"], SP * i)
                for n in range(2):
                    for t in range(2):
                        for g in range(2):
                            tt = 2 * n + t
                            o = t * CT + g * P
                            mm = pe.matmul(ps[:, BS0 + n, o:o + P], x_in[:, g, tt * P:(tt + 1) * P],
                                           w["mix"][:, g, :], start=True, stop=True)
                    mm.then_inc(s["h_ready"], 1)
                for k, out in enumerate((ps[:, BX, 0:CT], ps[:, BX, CT:2 * CT], ps[:, BZ0, 0:CT])):
                    for tt in range(TT):
                        if k == 0 and tt % 2 == 0:
                            pe.wait_ge(s["h_low_done"], 2 * i + tt // 2 + 1)
                        mm = three(out, w["wcT_high"][:, tt, k, :], w["wcT_low"][:, tt, k, :],
                                   h_high[:, tt, :], h_low[:, tt, :], tt == 0, tt == TT - 1)
                    if k == 1:
                        mm.then_inc(s["q_ready"], 1)
                    if k == 2:
                        mm.then_inc(s["kv_ready"], 1)
                pe.wait_ge(s["kv_done"], 1 * i + 1)
                for g in range(2):
                    mm = pe.transpose(ps[:, BZ0 + 1, g * P:(g + 1) * P], kv[:, g * P:(g + 1) * P], w["ident"][:])
                mm.then_inc(s["ct_ready"], 1)

            def fold(i, first):
                pe.wait_ge(s["q_done"], 2 * i + 2)
                for p in range(NPAIR):
                    if not (first and p < 2):
                        pe.wait_ge(s["qt_done"], NH * i + 2 * (p - 1))
                    for j in range(2):
                        h = 2 * p + j
                        out = ps[:, BT0 + p % 2, j * CT:(j + 1) * CT]
                        cols = slice((h % 4) * P, (h % 4 + 1) * P)
                        pe.matmul(out, w["m0_high"][:, h // 4, cols], q0_high[:], start=True, stop=False)
                        pe.matmul(out, w["m0_high"][:, h // 4, cols], q0_low[:], start=False, stop=False)
                        pe.matmul(out, w["m0_low"][:, h // 4, cols], q0_high[:], start=False, stop=False)
                        pe.matmul(out, w["m1"][:, h // 4, cols], q1_high[:], start=False, stop=False)
                        mm = pe.matmul(out, w["m1"][:, h // 4, cols], q1_low[:], start=False, stop=True)
                    mm.then_inc(s["t_ready"], 1)

            def scores(i, first):
                pe.wait_ge(s["qt_done"], NH * i + NH)
                for n in range(SP):
                    if n >= 2:
                        pe.wait_ge(s["s_taken"], SP * i + n - 1)
                    else:
                        pe.wait_ge(s["h_low_done"], 2 * i + 2)
                    for b in range(2):
                        tok = slice((2 * n + b) * C, (2 * n + b + 1) * C)
                        for j in range(4):
                            mm = pe.matmul(ps[32 * j:32 * j + 32, BS0 + n % 2, b * 256:(b + 1) * 256],
                                           kv[:, tok], qt[:, j:NH:4, tok], start=True, stop=True)
                    mm.then_inc(s["s_ready"], 1)

            def values(i, first, last):
                pe.wait_ge(s["c_loaded"], 128 * i + 128)
                for b in range(CB):
                    if b % 2 == 0:
                        pe.wait_ge(s["pl_done"], SP * i + b // 2 + 1)
                    if b >= 2:
                        pe.wait_ge(s["zl_done"], CB * i + b - 1)
                    elif b == 0 and not last:
                        pe.wait_ge(s["ct_done"], 1 * i + 2)
                    for p in range(2):
                        mm = three(ps[:, BZ0 + b % 2, p * 256:(p + 1) * 256], w["c_high"][:, b, p, :],
                                   w["c_low"][:, b, p, :],
                                   pT_high[:, b, :, :].rearrange("p a n -> p (a n)"),
                                   pT_low[:, b, :, :].rearrange("p a n -> p (a n)"))
                    mm.then_inc(s["z_ready"], 1)
                pe.wait_ge(s["zl_done"], CB * i + CB)
                if not first:
                    pe.wait_ge(s["o_done"], 1 * i)
                for p in range(NPAIR):
                    mm = three(ps[:, BO, 0:CT], w["wvT_high"][:, p, :], w["wvT_low"][:, p, :],
                               z_high[:, p % 2, p // 2, :], z_low[:, p % 2, p // 2, :], p == 0, p == NPAIR - 1)
                mm.then_inc(s["o_ready"], 1)

            front(0, True)
            fold(0, True)
            scores(0, True)
            front(1, False)
            fold(1, False)
            values(0, True, False)
            scores(1, False)
            front(2, False)
            with pe.Fori(2, NCH - 1) as i:
                fold(i, False)
                values(i - 1, False, False)
                scores(i, False)
                front(i + 1, False)
            fold(NCH - 1, False)
            values(NCH - 2, False, False)
            scores(NCH - 1, False)
            values(NCH - 1, False, True)

        @block.scalar
        def _(act):
            def front(i, first=False):
                for n in range(2):
                    act.wait_ge(s["h_ready"], 2 * i + n + 1)
                    act.copy(h_high[:, 2 * n:2 * n + 2, :].rearrange("p a n -> p (a n)"),
                             ps[:, BS0 + n, :]).then_inc(s["h_high_done"], 1)
                act.wait_ge(s["q_ready"], 1 * i + 1)
                act.activation(q0_high[:], ps[:, BX, 0:CT], ACT.Identity,
                               bias=w["bq_c"][:, 0:1]).then_inc(s["q_high_done"], 1)
                act.activation(q1_high[:], ps[:, BX, CT:2 * CT], ACT.Identity,
                               bias=w["bq_c"][:, 1:2]).then_inc(s["q_high_done"], 1)
                act.wait_ge(s["kv_ready"], 1 * i + 1)
                act.activation(kv[:], ps[:, BZ0, 0:CT], ACT.Identity, bias=w["bkv_c"][:, 0:1]).then_inc(s["kv_done"], 1)
                act.wait_ge(s["ct_ready"], 1 * i + 1)
                if not first:
                    act.wait_ge(s["c_stored"], 16 * i)
                act.copy(ctok[:, 0], ps[:, BZ0 + 1, 0:2 * P].rearrange("p (g c) -> p g c", g=2)[:, :, 0:64]
                         ).then_inc(s["ct_high_done"], 1)

            def fold(i, p0, p1):
                for p in range(p0, p1):
                    act.wait_ge(s["t_ready"], NPAIR * i + p + 1)
                    for j in range(2):
                        h = 2 * p + j
                        act.activation(qt[:, h, :], ps[:, BT0 + p % 2, j * CT:(j + 1) * CT], ACT.Identity,
                                       bias=w["m_bias"][:, h:h + 1]).then_inc(s["qt_done"], 1)

            def soft(i, n):
                act.wait_ge(s["sub_done"], SP * i + n + 1)
                v = sc[:, 2 * n:2 * n + 2, :, :].rearrange("p b a n -> p (b a n)")
                act.activation(v, v, ACT.Exp, scale=SCALE).then_inc(s["exp_done"], 1)

            def prob(i, n):
                act.wait_ge(s["turn_done"], SP * i + n + 1)
                act.copy(pT_high[:, 2 * n:2 * n + 2, :, :].rearrange("p b a n -> p (b a n)"),
                         pT[:, 2 * n:2 * n + 2, :, :].rearrange("p b a n -> p (b a n)")).then_inc(s["ph_done"], 1)

            def values(i):
                for b in range(CB):
                    act.wait_ge(s["z_ready"], CB * i + b + 1)
                    act.copy(z_high[:, :, :, b * C:(b + 1) * C],
                             ps[:, BZ0 + b % 2, :].rearrange("p (e a n) -> p e a n", e=2, a=QUADS)
                             ).then_inc(s["zh_done"], 1)

            def output(i):
                act.wait_ge(s["o_ready"], 1 * i + 1)
                act.activation(w["o_sum"][:, :, bass.ts(i, CB)].rearrange("p c b -> p b c"),
                               ps[:, BO, 0:CT].rearrange("p (b c) -> p b c", b=CB), ACT.Identity,
                               bias=w["bv_sum"][:, 0:1]).then_inc(s["o_done"], 1)

            def soft_and_fold(i):
                for n in range(SP):
                    soft(i - 1, n)
                    fold(i, 2 * n, 2 * n + 2)
                for n in range(SP):
                    prob(i - 1, n)
                    fold(i, 2 * SP + 2 * n, 2 * SP + 2 * n + 2)

            front(0, True)
            fold(0, 0, NPAIR)
            front(1)
            with act.Fori(1, NCH - 1) as i:
                soft_and_fold(i)
                values(i - 1)
                output(i - 1)
                front(i + 1)
            soft_and_fold(NCH - 1)
            values(NCH - 2)
            output(NCH - 2)
            for n in range(SP):
                soft(NCH - 1, n)
            for n in range(SP):
                prob(NCH - 1, n)
            values(NCH - 1)
            output(NCH - 1)
            act.wait_ge(s["o_done"], NCH)

        @block.vector
        def _(dve):
            def front(i, first):
                for n in range(2):
                    dve.wait_ge(s["h_high_done"], 2 * i + n + 1)
                    dve.tensor_tensor(h_low[:, 2 * n:2 * n + 2, :].rearrange("p a n -> p (a n)"), ps[:, BS0 + n, :],
                                      f(h_high[:, 2 * n:2 * n + 2, :].rearrange("p a n -> p (a n)")),
                                      ALU.subtract).then_inc(s["h_low_done"], 1)
                dve.wait_ge(s["q_high_done"], 2 * i + 2)
                for k, (hi, lo) in enumerate(((q0_high, q0_low), (q1_high, q1_low))):
                    dve.scalar_tensor_tensor(out=lo[:], in0=ps[:, BX, k * CT:(k + 1) * CT],
                                             scalar=w["bq_c"][:, k:k + 1], in1=f(hi[:]), op0=ALU.add,
                                             op1=ALU.subtract).then_inc(s["q_done"], 1)
                dve.wait_ge(s["ct_high_done"], 1 * i + 1)
                dve.tensor_tensor(ctok[:, 1], ps[:, BZ0 + 1, 0:2 * P].rearrange("p (g c) -> p g c", g=2)[:, :, 0:64],
                                  f(ctok[:, 0]), ALU.subtract).then_inc(s["ct_done"], 1)

            def take_scores(i):
                for n in range(SP):
                    dve.wait_ge(s["s_ready"], SP * i + n + 1)
                    dve.transpose(sc[:, 2 * n:2 * n + 2, :, :].rearrange("p b a n -> p (b a n)"),
                                  ps[:, BS0 + n % 2, :]).then_inc(s["s_taken"], 1)

            def softmax(i):
                part = lambda n: slice(2 * n, 2 * n + 2)
                wide = lambda ap: ap.unsqueeze(3).broadcast_to([P, 2, QUADS, C])
                for n in range(SP):
                    dve.wait_ge(s["s_taken"], SP * i + n + 1)
                    dve.tensor_reduce(row_max[:, part(n), :], sc[:, part(n), :, :], AX.X, ALU.max).then_inc(s["max_done"], 1)
                    dve.wait_ge(s["max_done"], SP * i + n + 1)
                    dve.tensor_tensor(sc[:, part(n), :, :], sc[:, part(n), :, :], wide(row_max[:, part(n), :]),
                                      ALU.subtract).then_inc(s["sub_done"], 1)
                for n in range(SP):
                    dve.wait_ge(s["exp_done"], SP * i + n + 1)
                    dve.tensor_reduce(row_sum[:, part(n), :], sc[:, part(n), :, :], AX.X, ALU.add).then_inc(s["sum_done"], 1)
                    dve.wait_ge(s["sum_done"], SP * i + n + 1)
                    dve.reciprocal(row_inv[:, part(n), :], row_sum[:, part(n), :]).then_inc(s["inv_done"], 1)
                    dve.wait_ge(s["inv_done"], SP * i + n + 1)
                    dve.tensor_tensor(sc[:, part(n), :, :], sc[:, part(n), :, :], wide(row_inv[:, part(n), :]),
                                      ALU.mult).then_inc(s["norm_done"], 1)
                    dve.wait_ge(s["norm_done"], SP * i + n + 1)
                    dve.transpose(pT[:, part(n), :, :].rearrange("p b a n -> p (b a n)"),
                                  sc[:, part(n), :, :].rearrange("p b a n -> p (b a n)")).then_inc(s["turn_done"], 1)
                for n in range(SP):
                    dve.wait_ge(s["ph_done"], SP * i + n + 1)
                    v = lambda t: t[:, part(n), :, :].rearrange("p b a n -> p (b a n)")
                    dve.tensor_tensor(v(pT_low), v(pT), f(v(pT_high)), ALU.subtract).then_inc(s["pl_done"], 1)

            def values(i, last=False):
                for b in range(CB):
                    dve.wait_ge(s["zh_done"], CB * i + b + 1)
                    if b == 0:
                        dve.wait_ge(s["pl_done"], SP * i + SP)
                    if b == 0 and not last:
                        dve.wait_ge(s["c_stored"], 16 * i + 32)
                    sl = slice(b * C, (b + 1) * C)
                    dve.tensor_tensor(z_low[:, :, :, sl],
                                      ps[:, BZ0 + b % 2, :].rearrange("p (e a n) -> p e a n", e=2, a=QUADS),
                                      f(z_high[:, :, :, sl]), ALU.subtract).then_inc(s["zl_done"], 1)

            front(0, True)
            take_scores(0)
            front(1, False)
            with dve.Fori(1, NCH - 1) as i:
                softmax(i - 1)
                values(i - 1)
                take_scores(i)
                front(i + 1, False)
            softmax(NCH - 2)
            values(NCH - 2)
            take_scores(NCH - 1)
            softmax(NCH - 1)
            values(NCH - 1, True)

    m.free()


def accurate_exp(dve, chain, x, n, k, e2, poly):
    chain(dve.tensor_scalar(x, x, -87.0, 88.3, ALU.max, ALU.min))
    chain(dve.tensor_scalar(k, x, LOG2E, MAGIC, ALU.mult, ALU.add))
    chain(dve.tensor_scalar(k, k, MAGIC, None, ALU.subtract))
    chain(dve.scalar_tensor_tensor(out=x, in0=k, scalar=-LN2_HI, in1=x, op0=ALU.mult, op1=ALU.add))
    chain(dve.scalar_tensor_tensor(out=x, in0=k, scalar=-LN2_LO, in1=x, op0=ALU.mult, op1=ALU.add))
    chain(dve.tensor_scalar(poly, x, 1.0 / math.factorial(8), None, ALU.mult))
    for c in range(7, 0, -1):
        chain(dve.scalar_tensor_tensor(out=poly, in0=poly, scalar=1.0 / math.factorial(c), in1=x,
                                       op0=ALU.add, op1=ALU.mult))
    chain(dve.tensor_scalar(e2, k, 127.0, None, ALU.add))
    chain(dve.tensor_scalar(e2, e2, 23, None, ALU.logical_shift_left))
    two_k = e2.bitcast(F32)
    chain(dve.scalar_tensor_tensor(out=k, in0=poly, scalar=1.0, in1=two_k, op0=ALU.add, op1=ALU.mult))
    chain(dve.tensor_tensor(poly, poly, two_k, ALU.mult))
    chain(dve.scalar_tensor_tensor(out=poly, in0=two_k, scalar=-1.0, in1=poly, op0=ALU.add, op1=ALU.add))


def reduce_angle(dve, chain, theta, k, quarter=None, quarter_rad=None):
    if quarter is None:
        chain(dve.tensor_scalar(k, theta, INV_2PI, MAGIC, ALU.mult, ALU.add))
    else:
        chain(dve.scalar_tensor_tensor(out=k, in0=theta, scalar=INV_2PI, in1=quarter, op0=ALU.mult, op1=ALU.add))
        chain(dve.tensor_scalar(k, k, MAGIC, None, ALU.add))
    chain(dve.tensor_scalar(k, k, MAGIC, None, ALU.subtract))
    for part in (PI_HI, PI_MID, PI_LO):
        chain(dve.scalar_tensor_tensor(out=theta, in0=k, scalar=-part, in1=theta, op0=ALU.mult, op1=ALU.add))
    if quarter is not None:
        chain(dve.tensor_tensor(theta, theta, quarter_rad, ALU.add))
    chain(dve.tensor_scalar(k, theta, INV_2PI, MAGIC, ALU.mult, ALU.add))
    chain(dve.tensor_scalar(k, k, MAGIC, -2 * math.pi, ALU.subtract, ALU.mult))
    chain(dve.tensor_tensor(theta, theta, k, ALU.add))
    chain(dve.tensor_scalar(theta, theta, -PI_IN, PI_IN, ALU.max, ALU.min))


def convolution_weights(nc, d, w, v, ps, scratch):
    m = Memory(nc)
    log_in = m.sb("log_in", [C, NMODE + 1])
    a_imag = m.sb("a_imag", [C, NMODE])
    c_in = m.sb("c_in", [C, NMODE, 2])
    d_row = m.sb("d_row", [1, C])
    ek = m.sb("ek", [C, NMODE + 1])
    ei = m.sb("ei", [C, NMODE + 1], I32)
    ep = m.sb("ep", [C, NMODE + 1])
    xk = m.sb("xk", [C, NMODE])
    xp = m.sb("xp", [C, NMODE])
    xr = m.sb("xr", [C, NMODE])
    ang = m.sb("ang", [C, NMODE])
    kk = m.sb("kk", [C, NMODE])
    sin1 = m.sb("sin1", [C, NMODE])
    sin2 = m.sb("sin2", [C, NMODE])
    t1 = m.sb("t1", [C, NMODE])
    t2 = m.sb("t2", [C, NMODE])
    w_re = m.sb("w_re", [C, NMODE])
    w_im = m.sb("w_im", [C, NMODE])
    q_re = m.sb("q_re", [C, NMODE])
    q_im = m.sb("q_im", [C, NMODE])
    par = m.sb("par", [C, 4, 2 * NMODE])
    parT = m.sb("parT", [P, 4, C])
    NL = 2 * LA + LC
    pos = m.sb("pos", [P, NL])
    quarter = m.sb("quarter", [P, NL])
    quarter_rad = m.sb("quarter_rad", [P, NL])
    theta = m.sb("theta", [P, C, NL])
    turns = m.sb("turns", [P, C, NL])
    decay = m.sb("decay", [P, C, NL])
    g_t = m.sb("g_t", [P, C, LA])
    taps = m.sb("taps", [LA, C, LC])
    zero = m.sb("zero", [C, KPAD])
    qw = m.sb("qw", [P, TT, 3 * P], I32)
    un = m.sb("un", [P, TT, P, 4], I32)
    wf = m.sb("wf", [P, TT, T])
    zp = m.sb("zp", [P, TT])
    wsc = m.sb("wsc", [P, TT])
    wo_raw = m.sb("wo_raw", [P, TT, VH])
    len_i = m.sb("len_i", [P, B], I32)
    len_f = m.sb("len_f", [P, B])
    l_pos = m.sb("l_pos", [P, 1])

    s_names = ("ssm_in ffn_in wo_in len_in step const_ready exp_go exp_done sin_go sin_done par_ready par_turned "
               "gf_ready taps_ready taps_done taps_stored zero_ready wf_ready wfT_ready wfT_high wfT_done woT_ready "
               "woT_high woT_done").split()
    s = {n: m.sem(n) for n in s_names}

    with nc.Block() as block:

        @block.sync
        def _(sp):
            sp.dma_start(log_in[:, 0:NMODE], d["L0_cond2_log_A_real"]).then_inc(s["ssm_in"], 16)
            sp.dma_start(log_in[:, NMODE:NMODE + 1], d["L0_cond2_log_dt"].rearrange("(p a) -> p a", a=1)).then_inc(s["ssm_in"], 16)
            sp.dma_start(a_imag[:], d["L0_cond2_A_imag"]).then_inc(s["ssm_in"], 16)
            sp.dma_start(c_in[:], d["L0_cond2_C"]).then_inc(s["ssm_in"], 16)
            sp.dma_start(d_row[:], d["L0_cond2_D"].rearrange("(a p) -> a p", a=1)).then_inc(s["ssm_in"], 16)
            sp.dma_start(v["bo"][:], d["L0_attn_bo"].partition_broadcast(P)).then_inc(v["bias_in"], 16)
            sp.dma_start(v["fb"][:], d["L0_ffn_bias"].partition_broadcast(P)).then_inc(v["bias_in"], 16)
            k_out = scratch["taps"][:, KPAD:KPAD + T].rearrange("h (a c) -> a h c", a=LA)
            sp.wait_ge(s["zero_ready"], 1)
            sp.dma_start(scratch["taps"][:, 0:KPAD], zero[:]).then_inc(s["taps_stored"], 16)
            sp.wait_ge(s["taps_done"], 3)
            sp.dma_start(k_out, taps[:]).then_inc(s["taps_stored"], 16)
            sp.wait_ge(s["taps_stored"], 32)
            sp.wait_ge(v["bias_in"], 32)

        @block.gpsimd
        def _(pool):
            pool.memset(zero[:], 0.0).then_inc(s["zero_ready"], 1)
            pool.iota(pos[:, 0:2 * LA], pattern=[[0, 2], [LC, LA]], base=0, channel_multiplier=0,
                      allow_small_or_imprecise_dtypes=True).then_inc(s["const_ready"], 1)
            pool.iota(pos[:, 2 * LA:NL], pattern=[[1, LC]], base=0, channel_multiplier=0,
                      allow_small_or_imprecise_dtypes=True).then_inc(s["const_ready"], 1)
            pool.iota(l_pos[:], pattern=[[0, 1]], base=0, channel_multiplier=1,
                      allow_small_or_imprecise_dtypes=True).then_inc(s["const_ready"], 1)
            for n, (tile, value) in enumerate(((quarter, 0.25), (quarter_rad, math.pi / 2))):
                pool.memset(tile[:, 0:LA], value).then_inc(s["const_ready"], 1)
                pool.memset(tile[:, LA:NL], 0.0).then_inc(s["const_ready"], 1)
                pool.wait_ge(s["const_ready"], 3 + 3 * n + 2)
                pool.memset(tile[0:64, 2 * LA:NL], value).then_inc(s["const_ready"], 1)
                pool.wait_ge(s["const_ready"], 3 + 3 * n + 3)

        @block.tensor
        def _(pe):
            pe.wait_ge(s["wo_in"], 16)
            for t in range(TT):
                mm = pe.transpose(ps[:, 4, t * P:(t + 1) * P], wo_raw[:, t, :], w["ident"][:])
            mm.then_inc(s["woT_ready"], 1)
            pe.wait_ge(s["wf_ready"], TT)
            for t in range(TT):
                for n in range(TT):
                    mm = pe.transpose(ps[:, t, n * P:(n + 1) * P], wf[:, n, t * P:(t + 1) * P], w["ident"][:])
                mm.then_inc(s["wfT_ready"], 1)
            pe.wait_ge(s["par_ready"], 1)
            for n in range(4):
                mm = pe.transpose(ps[:, 5, n * C:(n + 1) * C], par[:, n, :], w["ident"][0:C, 0:C])
            mm.then_inc(s["par_turned"], 1)
            pe.wait_ge(s["gf_ready"], 1)
            for h in range(C):
                mm = pe.matmul(ps[0:LA, 6 + h // 16, (h % 16) * LC:(h % 16 + 1) * LC], g_t[:, h, :],
                               theta[:, h, 2 * LA:NL], start=True, stop=True)
                if h % 16 == 15:
                    mm.then_inc(s["taps_ready"], 1)

        @block.scalar
        def _(act):
            act.dma_start(qw[:], d["L0_ffn_qweight"].rearrange("(t n) k -> n t k", n=P)).then_inc(s["ffn_in"], 16)
            act.dma_start(zp[:], d["L0_ffn_weight_zero_point"].rearrange("(t n) a -> n (t a)", n=P), allow_slow_non_contiguous=True).then_inc(s["ffn_in"], 16)
            act.dma_start(wsc[:], d["L0_ffn_weight_scale"].rearrange("(t n) a -> n (t a)", n=P), allow_slow_non_contiguous=True).then_inc(s["ffn_in"], 16)
            act.dma_start(wo_raw[:], d["L0_attn_Wo"].rearrange("(t n) k -> n t k", n=P)).then_inc(s["wo_in"], 16)
            act.dma_start(len_i[:], d["itok_B_8_3872"].partition_broadcast(P)).then_inc(s["len_in"], 16)
            act.wait_ge(s["woT_ready"], 1)
            act.copy(v["woT_high"][:], ps[:, 4, :]).then_inc(s["woT_high"], 1)
            for t in range(TT):
                act.wait_ge(s["wfT_ready"], t + 1)
                act.copy(v["wfT_high"][:, t, :], ps[:, t, :]).then_inc(s["wfT_high"], 1)
            act.wait_ge(s["sin_go"], 1)
            act.activation(sin1[:], ang[:], ACT.Sin).then_inc(s["sin_done"], 1)
            act.activation(sin2[:], ang[:], ACT.Sin, scale=0.5).then_inc(s["sin_done"], 1)
            act.wait_ge(s["sin_go"], 2)
            act.activation(theta[:], theta[:], ACT.Sin).then_inc(s["sin_done"], 1)
            act.wait_ge(s["exp_go"], 1)
            act.activation(decay[:], decay[:], ACT.Exp).then_inc(s["exp_done"], 1)

        @block.vector
        def _(dve):
            steps = [0]

            def chain(ins):
                steps[0] += 1
                ins.then_inc(s["step"], 1)
                dve.wait_ge(s["step"], steps[0])

            dve.wait_ge(s["ffn_in"], 48)
            pk = qw[:].rearrange("p t (g e) -> p (t g) e", e=3)
            uv = un[:].rearrange("p t g e -> p (t g) e")
            dve.tensor_scalar(uv[:, :, 0], pk[:, :, 0], 63, None, ALU.bitwise_and)
            dve.tensor_scalar(uv[:, :, 1], pk[:, :, 0], 6, 63, ALU.logical_shift_right, ALU.bitwise_and)
            dve.tensor_scalar(uv[:, :, 2], pk[:, :, 1], 63, None, ALU.bitwise_and)
            chain(dve.tensor_scalar(uv[:, :, 3], pk[:, :, 2], 63, None, ALU.bitwise_and))
            for t in range(TT):
                dve.tensor_scalar(wf[:, t, :], un[:, t, :, :].rearrange("p g e -> p (g e)"), zp[:, t:t + 1],
                                  wsc[:, t:t + 1], ALU.subtract, ALU.mult).then_inc(s["wf_ready"], 1)
            dve.wait_ge(s["woT_high"], 1)
            dve.tensor_tensor(v["woT_low"][:], ps[:, 4, :], f(v["woT_high"][:]), ALU.subtract).then_inc(s["woT_done"], 1)
            for t in range(TT):
                dve.wait_ge(s["wfT_high"], t + 1)
                dve.tensor_tensor(v["wfT_low"][:, t, :], ps[:, t, :], f(v["wfT_high"][:, t, :]),
                                  ALU.subtract).then_inc(s["wfT_done"], 1)
            dve.wait_ge(s["len_in"], 16)
            dve.wait_ge(s["const_ready"], 9)
            chain(dve.tensor_copy(len_f[:], len_i[:]))
            for t in range(TT):
                chain(dve.tensor_scalar(v["mask"][:, t, :], len_f[:], l_pos[:, 0:1], float(P * t), ALU.subtract, ALU.is_gt))
            dve.wait_ge(s["ssm_in"], 80)
            accurate_exp(dve, chain, log_in[:], NMODE + 1, ek[:], ei[:], ep[:])
            ea, dt = ek[:, 0:NMODE], ek[:, NMODE:NMODE + 1]
            dta_re, dta_im = par[:, 0, 0:NMODE], par[:, 1, 0:NMODE]
            chain(dve.tensor_scalar(dta_re, ea, dt, -1.0, ALU.mult, ALU.mult))
            chain(dve.tensor_scalar(dta_im, a_imag[:], dt, None, ALU.mult))
            dve.tensor_copy(par[:, 0, NMODE:], dta_re)
            dve.tensor_copy(par[:, 1, NMODE:], dta_im)
            dve.tensor_copy(xr[:], dta_re)
            chain(dve.tensor_copy(ang[:], dta_im))
            accurate_exp(dve, chain, xr[:], NMODE, xk[:], ei[:, 0:NMODE], xp[:])
            reduce_angle(dve, chain, ang[:], kk[:])
            dve.sem_inc(s["sin_go"], 1)
            dve.wait_ge(s["sin_done"], 2)
            chain(dve.tensor_tensor(t1[:], sin2[:], sin2[:], ALU.mult))
            chain(dve.tensor_tensor(t1[:], t1[:], xk[:], ALU.mult))
            chain(dve.scalar_tensor_tensor(out=w_re[:], in0=t1[:], scalar=-2.0, in1=xp[:], op0=ALU.mult, op1=ALU.add))
            chain(dve.tensor_tensor(w_im[:], sin1[:], xk[:], ALU.mult))
            chain(dve.tensor_tensor(t1[:], ea, ea, ALU.mult))
            chain(dve.tensor_tensor(t2[:], a_imag[:], a_imag[:], ALU.mult))
            chain(dve.tensor_tensor(t1[:], t1[:], t2[:], ALU.add))
            chain(dve.reciprocal(kk[:], t1[:]))
            chain(dve.tensor_tensor(t1[:], w_im[:], a_imag[:], ALU.mult))
            chain(dve.tensor_tensor(t2[:], w_re[:], ea, ALU.mult))
            chain(dve.tensor_tensor(t1[:], t1[:], t2[:], ALU.subtract))
            chain(dve.tensor_tensor(q_re[:], t1[:], kk[:], ALU.mult))
            chain(dve.tensor_tensor(t1[:], w_re[:], a_imag[:], ALU.mult))
            chain(dve.tensor_tensor(t2[:], w_im[:], ea, ALU.mult))
            chain(dve.tensor_tensor(t1[:], t1[:], t2[:], ALU.add))
            chain(dve.scalar_tensor_tensor(out=q_im[:], in0=t1[:], scalar=-1.0, in1=kk[:], op0=ALU.mult, op1=ALU.mult))
            chain(dve.tensor_tensor(t1[:], c_in[:, :, 0], q_re[:], ALU.mult))
            chain(dve.tensor_tensor(t2[:], c_in[:, :, 1], q_im[:], ALU.mult))
            chain(dve.tensor_tensor(w_re[:], t1[:], t2[:], ALU.subtract))
            chain(dve.tensor_tensor(t1[:], c_in[:, :, 0], q_im[:], ALU.mult))
            chain(dve.tensor_tensor(t2[:], c_in[:, :, 1], q_re[:], ALU.mult))
            chain(dve.tensor_tensor(w_im[:], t1[:], t2[:], ALU.add))
            dve.tensor_scalar(par[:, 2, 0:NMODE], w_re[:], 2.0, None, ALU.mult)
            dve.tensor_scalar(par[:, 2, NMODE:], w_im[:], -2.0, None, ALU.mult)
            dve.tensor_scalar(par[:, 3, 0:NMODE], w_im[:], -2.0, None, ALU.mult)
            dve.tensor_scalar(par[:, 3, NMODE:], w_re[:], -2.0, None, ALU.mult).then_inc(s["par_ready"], 1)
            dve.wait_ge(s["par_turned"], 1)
            chain(dve.tensor_copy(parT[:].rearrange("p a h -> p (a h)"), ps[:, 5, 0:4 * C]))
            by_h = lambda n, k: parT[:, n, :].unsqueeze(2).broadcast_to([P, C, k])
            by_l = lambda tile: tile[:].unsqueeze(1).broadcast_to([P, C, NL])
            chain(dve.tensor_tensor(theta[:], by_h(1, NL), by_l(pos), ALU.mult))
            dve.tensor_tensor(decay[:], by_h(0, NL), by_l(pos), ALU.mult).then_inc(s["exp_go"], 1)
            reduce_angle(dve, chain, theta[:], turns[:], by_l(quarter), by_l(quarter_rad))
            dve.sem_inc(s["sin_go"], 1)
            dve.wait_ge(s["sin_done"], 3)
            dve.wait_ge(s["exp_done"], 1)
            chain(dve.tensor_tensor(theta[:], theta[:], decay[:], ALU.mult))
            chain(dve.tensor_tensor(g_t[:], theta[:, :, 0:LA], by_h(2, LA), ALU.mult))
            chain(dve.tensor_tensor(turns[:, :, 0:LA], theta[:, :, LA:2 * LA], by_h(3, LA), ALU.mult))
            dve.tensor_tensor(g_t[:], g_t[:], turns[:, :, 0:LA], ALU.add).then_inc(s["gf_ready"], 1)
            for n in range(2):
                dve.wait_ge(s["taps_ready"], n + 1)
                dve.tensor_copy(taps[:, 16 * n:16 * n + 16, :].rearrange("a h c -> a (h c)"),
                                ps[0:LA, 6 + n, :]).then_inc(s["taps_done"], 1)
            dve.wait_ge(s["taps_done"], 2)
            dve.tensor_tensor(taps[0:1, :, 0], taps[0:1, :, 0], d_row[:], ALU.add).then_inc(s["taps_done"], 1)
            dve.wait_ge(s["taps_done"], 3)
            dve.wait_ge(s["woT_done"], 1)
            dve.wait_ge(s["wfT_done"], TT)

    m.free()


def channels(nc, d, w, v, ps, scratch, out):
    m = Memory(nc)
    R = 4
    x_s = [m.sb(f"x_s{n}", [B, T]) for n in range(R)]
    toep = [m.sb(f"toep{n}", [P, T]) for n in range(R)]
    x1 = [m.sb(f"x1_{n}", [B, T]) for n in range(2)]
    o_high = [m.sb(f"o_high{n}", [VH, B], F32R) for n in range(2)]
    o_low = [m.sb(f"o_low{n}", [VH, B], F32R) for n in range(2)]
    x1T = [m.sb(f"x1T{n}", [P, TT, B]) for n in range(2)]
    y = [m.sb(f"y{n}", [P, TT, B]) for n in range(2)]
    y_high = [m.sb(f"y_high{n}", [P, TT, B], F32R) for n in range(2)]
    y_low = [m.sb(f"y_low{n}", [P, TT, B], F32R) for n in range(2)]
    res = [m.sb(f"res{n}", [B, T]) for n in range(2)]
    names = ("xb_done oh_done ol_done a_ready x1_done x1b_done b_ready x1T_done conv_ready y_done yh_done yl_done "
             "f_ready res_done").split()
    s = {n: m.sem(n) for n in names}
    x_in = [m.sem(f"x_in{n}") for n in range(R)]
    toep_in = [m.sem(f"toep_in{n}") for n in range(R)]
    stored = [m.sem(f"stored{n}") for n in range(2)]
    LAG = 3

    def backwards(tile):
        return tile[:].rearrange("b (t j) -> b t j", t=TT)[:, :, ::-1]

    def run(eng, step):
        for n in range(2 * R):
            step(n, n % R)
        with eng.Fori(2, C // R) as i:
            for n in range(R):
                step(i * R + n, n)
        for n in range(LAG):
            step(C + n, n)

    def on(c):
        return not isinstance(c, int) or 0 <= c < C

    def past(c, k):
        return not isinstance(c, int) or c >= k

    def rounds(c, u, ring):
        return c // ring + 1 if isinstance(c, int) else (c - u) // ring + 1

    with nc.Block() as block:

        @block.sync
        def _(sp):
            def load(c, u):
                if not on(c):
                    return
                if past(c, R):
                    sp.wait_ge(s["res_done"], c - R + 1)
                sp.dma_start(x_s[u][:], d["x"][:, bass.ds(c, 1), :].rearrange("b a t -> b (a t)")).then_inc(x_in[u], 16)
                taps = scratch["taps"]
                src = bass.AP(taps.tensor, c * KROW, [[1, P], [1, T]])
                sp.dma_start(toep[u][:], src).then_inc(toep_in[u], 16)

            def store(c, u):
                if not on(c):
                    return
                sp.wait_ge(s["res_done"], c + 1)
                sp.dma_start(out[:, bass.ds(c, 1), :].rearrange("b a t -> b (a t)"), res[u % 2][:]).then_inc(stored[u % 2], 16)

            def step(c, u):
                load(c, u)
                store(c - LAG, (u - LAG) % R)

            run(sp, step)
            for n in range(2):
                sp.wait_ge(stored[n], 16 * C // 2)

        @block.gpsimd
        def _(pool):
            def step(c, u):
                if on(c):
                    pool.wait_ge(x_in[u], 16 * rounds(c, u, R))
                    pool.tensor_tensor(x_s[u][:], x_s[u][:], v["bo"][:], ALU.add).then_inc(s["xb_done"], 1)
                if on(c - 1):
                    q = (u - 1) % R
                    pool.wait_ge(s["x1_done"], c)
                    if past(c - 1, 0):
                        pool.tensor_tensor(x_s[q][:].rearrange("b (t j) -> b t j", t=TT), backwards(x1[q % 2]),
                                           v["fb"][:].rearrange("b (t j) -> b t j", t=TT), ALU.add).then_inc(s["x1b_done"], 1)
                if on(c - 2):
                    q = (u - 2) % 2
                    pool.wait_ge(s["yh_done"], c - 1)
                    if past(c - 2, 2):
                        pool.wait_ge(s["f_ready"], c - 3)
                    pool.tensor_tensor(y_low[q][:], y[q][:], f(y_high[q][:]), ALU.subtract).then_inc(s["yl_done"], 1)

            run(pool, step)

        @block.tensor
        def _(pe):
            def step(c, u):
                if on(c):
                    q = u % 2
                    pe.wait_ge(s["ol_done"], c + 1)
                    if past(c, 2):
                        pe.wait_ge(s["x1_done"], c - 1)
                    a = ps[:, q, :]
                    pe.matmul(a, o_high[q][:], v["woT_high"][:], start=True, stop=False)
                    pe.matmul(a, o_high[q][:], v["woT_low"][:], start=False, stop=False)
                    pe.matmul(a, o_low[q][:], v["woT_high"][:], start=False, stop=True).then_inc(s["a_ready"], 1)
                if on(c - 1):
                    q = (u - 1) % 2
                    pe.wait_ge(s["x1_done"], c)
                    if past(c - 1, 2):
                        pe.wait_ge(s["x1T_done"], c - 2)
                    for t in range(TT):
                        mm = pe.transpose(ps[:, 2 + q, t * P:(t + 1) * P], x1[q][:, t * P:(t + 1) * P], w["ident"][:])
                    mm.then_inc(s["b_ready"], 1)
                if on(c - 2):
                    q, g = (u - 2) % 2, (u - 2) % R
                    pe.wait_ge(s["x1T_done"], c - 1)
                    pe.wait_ge(toep_in[g], 16 * rounds(c - 2, g, R))
                    if past(c - 2, 2):
                        pe.wait_ge(s["y_done"], c - 3)
                    for e in range(TT):
                        mm = pe.matmul(ps[:, 4 + q, e * P:T], toep[g][:, e * P:(e + 1) * P],
                                       x1T[q][:, 0:TT - e, :].rearrange("p t b -> p (t b)"), start=(e == 0),
                                       stop=(e == TT - 1))
                    mm.then_inc(s["conv_ready"], 1)
                if on(c - 3):
                    q = (u - 3) % 2
                    pe.wait_ge(s["yl_done"], c - 2)
                    if past(c - 3, 2):
                        pe.wait_ge(s["res_done"], c - 4)
                    for t in range(TT):
                        a = ps[:, 6 + q, :]
                        pe.matmul(a, y_high[q][:, t, :], v["wfT_high"][:, t, :], start=(t == 0), stop=False)
                        pe.matmul(a, y_high[q][:, t, :], v["wfT_low"][:, t, :], start=False, stop=False)
                        mm = pe.matmul(a, y_low[q][:, t, :], v["wfT_high"][:, t, :], start=False, stop=(t == TT - 1))
                    mm.then_inc(s["f_ready"], 1)

            run(pe, step)

        @block.scalar
        def _(act):
            def step(c, u):
                if on(c):
                    q = u % 2
                    if past(c, 2):
                        act.wait_ge(s["a_ready"], c - 1)
                    act.copy(o_high[q][:], w["o_sum"][:, bass.ds(c, 1), :].rearrange("p a b -> p (a b)")).then_inc(s["oh_done"], 1)
                if on(c - 1):
                    q = (u - 1) % 2
                    act.wait_ge(s["b_ready"], c)
                    if past(c - 1, 2):
                        act.wait_ge(s["conv_ready"], c - 2)
                    act.copy(x1T[q][:].rearrange("p t b -> p (t b)"), ps[:, 2 + q, :]).then_inc(s["x1T_done"], 1)
                if on(c - 2):
                    q = (u - 2) % 2
                    act.wait_ge(s["y_done"], c - 1)
                    if past(c - 2, 2):
                        act.wait_ge(s["f_ready"], c - 3)
                    act.copy(y_high[q][:], y[q][:]).then_inc(s["yh_done"], 1)

            run(act, step)

        @block.vector
        def _(dve):
            def step(c, u):
                if on(c):
                    q = u % 2
                    dve.wait_ge(s["oh_done"], c + 1)
                    dve.tensor_tensor(o_low[q][:], w["o_sum"][:, bass.ds(c, 1), :].rearrange("p a b -> p (a b)"),
                                      f(o_high[q][:]), ALU.subtract).then_inc(s["ol_done"], 1)
                    dve.wait_ge(s["a_ready"], c + 1)
                    dve.wait_ge(s["xb_done"], c + 1)
                    if past(c, 2):
                        dve.wait_ge(s["x1b_done"], c - 1)
                        dve.wait_ge(s["b_ready"], c - 1)
                    dve.tensor_tensor(backwards(x1[q]), ps[:, q, :].rearrange("b (t j) -> b t j", t=TT),
                                      x_s[u][:].rearrange("b (t j) -> b t j", t=TT), ALU.add).then_inc(s["x1_done"], 1)
                if on(c - 2):
                    q = (u - 2) % 2
                    dve.wait_ge(s["conv_ready"], c - 1)
                    if past(c - 2, 2):
                        dve.wait_ge(s["yl_done"], c - 3)
                    dve.tensor_tensor(y[q][:], ps[:, 4 + q, :].rearrange("p (t b) -> p t b", t=TT), v["mask"][:],
                                      ALU.mult).then_inc(s["y_done"], 1)
                if on(c - 3):
                    q, g = (u - 3) % 2, (u - 3) % R
                    dve.wait_ge(s["f_ready"], c - 2)
                    dve.wait_ge(s["x1b_done"], c - 2)
                    if past(c - 3, 2):
                        dve.wait_ge(stored[q], (c - 3 - q) * 8)
                    dve.tensor_tensor(res[q][:], ps[:, 6 + q, :], x_s[g][:], ALU.add).then_inc(s["res_done"], 1)

            run(dve, step)

    m.free()


def build(nc, d, out):
    whole = Memory(nc)
    scratch = {
        "mix": nc.dram_tensor("mix_scratch", (B, C * C), F32, kind="Internal").ap(),
        "lat": nc.dram_tensor("lat_scratch", (B * C, 2, KVL), F32, kind="Internal").ap(),
        "taps": nc.dram_tensor("taps_scratch", (C, KROW), F32, kind="Internal").ap(),
    }
    ps = whole.ctx.enter_context(nc.psum_tensor("ps", [P, 8, 512], F32))
    w = {"ident": whole.sb("ident", [P, P]), "o_sum": whole.sb("o_sum", [VH, C, B])}
    first = Memory(nc)
    for name, shape, dt in (
            ("mix", [P, 2, P], F32), ("bq_c", [P, 2], F32), ("bkv_c", [P, 1], F32), ("m_bias", [P, NH], F32),
            ("bv_sum", [P, 1], F32), ("wcT_high", [P, TT, 3, P], F32R), ("wcT_low", [P, TT, 3, P], F32R),
            ("m0_high", [P, QUADS, 4 * P], F32R), ("m0_low", [P, QUADS, 4 * P], F32R), ("m1", [P, QUADS, 4 * P], F32R),
            ("wvT_high", [P, NPAIR, P], F32R), ("wvT_low", [P, NPAIR, P], F32R),
            ("c_high", [P, CB, 2, P], F32R), ("c_low", [P, CB, 2, P], F32R)):
        w[name] = first.sb(name, shape, dt)
    attention_weights(nc, d, w, ps, scratch)
    attention(nc, d, w, ps, scratch)
    first.free()
    second = Memory(nc)
    v = {"bias_in": second.sem("ffn_bias_in")}
    for name, shape, dt in (
            ("bo", [P, T], F32), ("fb", [P, T], F32), ("mask", [P, TT, B], F32), ("woT_high", [VH, T], F32R),
            ("woT_low", [VH, T], F32R), ("wfT_high", [P, TT, T], F32R), ("wfT_low", [P, TT, T], F32R)):
        v[name] = second.sb(name, shape, dt)
    convolution_weights(nc, d, w, v, ps, scratch)
    channels(nc, d, w, v, ps, scratch, out)
    second.free()
    whole.free()


NAMES = ["x", "itok_B_0_15", "itok_B_8_3872", "L0_cond_weights", "L0_attn_Wq_c", "L0_attn_bq_c", "L0_attn_Wq_up",
         "L0_attn_bq_up", "L0_attn_Wkv_c", "L0_attn_bkv_c", "L0_attn_Wkv_up", "L0_attn_bkv_up", "L0_attn_Wo",
         "L0_attn_bo", "L0_cond2_log_dt", "L0_cond2_C", "L0_cond2_log_A_real", "L0_cond2_A_imag", "L0_cond2_D",
         "L0_ffn_qweight", "L0_ffn_weight_scale", "L0_ffn_weight_zero_point", "L0_ffn_bias"]


def kernel(**inputs):
    import numpy as np
    import concourse.bacc as bacc
    from concourse.bass_utils import run_bass_kernel_spmd

    nc = bacc.Bacc("TRN2", target_bir_lowering=False, num_devices=1)
    arrays, d = {}, {}
    for name in NAMES:
        a = np.ascontiguousarray(inputs[name])
        arrays[f"in_{name}"] = a
        d[name] = nc.dram_tensor(f"in_{name}", a.shape, mybir.dt.from_np(a.dtype), kind="ExternalInput").ap()
    out = nc.dram_tensor("out_0", (B, C, T), F32, kind="ExternalOutput").ap()
    build(nc, d, out)
    return run_bass_kernel_spmd(nc, [arrays], core_ids=[0]).results[0]["out_0"]
```
